# Optimizing a Trainium2 kernel written in Bass

```python
import numpy as np
import jax
import jax.numpy as jnp

def _softmax(x, axis=-1):
    return jax.nn.softmax(x, axis=axis)

def _gelu(x):
    return jax.nn.gelu(x, approximate=True)

def _silu(x):
    return jax.nn.silu(x)

def _sigmoid(x):
    return jax.nn.sigmoid(x)

def _layernorm(x, axis=-1, eps=1e-05):
    m = jnp.mean(x, axis=axis, keepdims=True)
    v = jnp.var(x, axis=axis, keepdims=True)
    return (x - m) / jnp.sqrt(v + eps)

def _scatter_add(tgt, idx, src, axis=0):
    return tgt.at[idx].add(src)

def _segment_sum(src, seg, n):
    return jax.ops.segment_sum(src, seg, n)
kernel_name = 'mk_sandwich_d1_jaxref_r8_3863aa'

def setup_inputs(seed: int=0):
    np.random.seed(seed)
    _w = jnp.asarray

    def _L0_attn_setup():
        import jax, jax.numpy as jnp
        import numpy as np
        D_MODEL = 128
        N_HEADS = 16
        D_HEAD = 64
        BATCH = 4
        SEQ = 256
        NEG = -1000000000.0
        key = jax.random.key(seed)
        k1, k2, k3, k4, k5 = jax.random.split(key, 5)
        x = jax.random.normal(k1, (BATCH, SEQ, D_MODEL), dtype=jnp.float32)
        std = 0.02
        wq = jax.random.normal(k2, (N_HEADS, D_HEAD, D_MODEL), dtype=jnp.float32) * std
        wk = jax.random.normal(k3, (N_HEADS, D_HEAD, D_MODEL), dtype=jnp.float32) * std
        wv = jax.random.normal(k4, (N_HEADS, D_HEAD, D_MODEL), dtype=jnp.float32) * std
        wo = jax.random.normal(k5, (D_MODEL, N_HEADS * D_HEAD), dtype=jnp.float32) * std
        return {'x': x, 'wq': wq, 'wk': wk, 'wv': wv, 'wo': wo}
    _L0_attn_in = _L0_attn_setup()

    def _L0_ffn_setup():
        import jax, jax.numpy as jnp
        import numpy as np
        DIM = 128
        HIDDEN = 384
        SCALE = 1.0 / 127.0

        def _dequant(w_int, dtype):
            return w_int.astype(dtype) * jnp.asarray(SCALE, dtype)
        key = jax.random.key(seed)
        k_x, k_g, k_u, k_d = jax.random.split(key, 4)
        x = jax.random.normal(k_x, (4, 256, DIM), dtype=jnp.float32)
        w_gate = jax.random.randint(k_g, (HIDDEN, DIM), -127, 128, dtype=jnp.int32)
        w_up = jax.random.randint(k_u, (HIDDEN, DIM), -127, 128, dtype=jnp.int32)
        w_down = jax.random.randint(k_d, (DIM, HIDDEN), -127, 128, dtype=jnp.int32)
        return {'x': x, 'w_gate': w_gate, 'w_up': w_up, 'w_down': w_down}
    _L0_ffn_in = _L0_ffn_setup()
    _d = {'L0_attn_x': _L0_attn_in['x'], 'L0_attn_wq': _L0_attn_in['wq'], 'L0_attn_wk': _L0_attn_in['wk'], 'L0_attn_wv': _L0_attn_in['wv'], 'L0_attn_wo': _L0_attn_in['wo'], 'L0_ffn_w_gate': _L0_ffn_in['w_gate'], 'L0_ffn_w_up': _L0_ffn_in['w_up'], 'L0_ffn_w_down': _L0_ffn_in['w_down']}
    _x0 = _d['L0_attn_x']
    _d['L0_attn_x'] = jax.random.normal(jax.random.fold_in(jax.random.key(seed), 1), (4, 1024, 128), dtype=_x0.dtype)
    del _x0
    return _d

def reference(L0_attn_x, L0_attn_wq, L0_attn_wk, L0_attn_wv, L0_attn_wo, L0_ffn_w_gate, L0_ffn_w_up, L0_ffn_w_down):

    def _L0_attn_ref(x, wq, wk, wv, wo):
        import jax, jax.numpy as jnp
        import numpy as np
        D_MODEL = 128
        N_HEADS = 16
        D_HEAD = 64
        BATCH = 4
        SEQ = 256
        NEG = -1000000000.0
        b, s, _ = x.shape
        scale = jnp.sqrt(jnp.asarray(D_HEAD, x.dtype))
        q = jnp.einsum('bsd,hed->bhse', x, wq)
        k = jnp.einsum('bsd,hed->bhse', x, wk)
        v = jnp.einsum('bsd,hed->bhse', x, wv)
        scores = jnp.einsum('bhse,bhte->bhst', q, k) / scale
        causal_mask = jnp.triu(jnp.ones((s, s), dtype=bool), k=1)
        scores = jnp.where(causal_mask, jnp.asarray(NEG, scores.dtype), scores)
        weights = jax.nn.softmax(scores, axis=-1)
        heads = jnp.einsum('bhst,bhte->bhse', weights, v)
        concat = heads.transpose(0, 2, 1, 3).reshape(b, s, N_HEADS * D_HEAD)
        return concat @ wo.T

    def _L0_ffn_ref(x, w_gate, w_up, w_down):
        import jax, jax.numpy as jnp
        import numpy as np
        DIM = 128
        HIDDEN = 384
        SCALE = 1.0 / 127.0

        def _dequant(w_int, dtype):
            return w_int.astype(dtype) * jnp.asarray(SCALE, dtype)
        wg = _dequant(w_gate, x.dtype)
        wu = _dequant(w_up, x.dtype)
        wd = _dequant(w_down, x.dtype)
        gate = jnp.einsum('bsd,hd->bsh', x, wg)
        up = jnp.einsum('bsd,hd->bsh', x, wu)
        h = jax.nn.silu(gate) * up
        return jnp.einsum('bsh,dh->bsd', h, wd)
    x = L0_attn_x
    x = x + _layernorm(_L0_attn_ref(_layernorm(x, axis=-1), L0_attn_wq, L0_attn_wk, L0_attn_wv, L0_attn_wo), axis=-1)
    x = x + _layernorm(_L0_ffn_ref(_layernorm(x, axis=-1), L0_ffn_w_gate, L0_ffn_w_up, L0_ffn_w_down), axis=-1)
    return x

_drawn_inputs = setup_inputs


def setup_inputs(seed=0):
    import zlib

    import numpy as np

    out = dict(_drawn_inputs(seed))
    spreads = {}
    factors = {}
    for name, (base, spread) in spreads.items():
        noise = np.random.default_rng([zlib.crc32(name.encode()), seed]).standard_normal(out[name].shape)
        drawn = base * np.exp(spread * noise) if base else spread * noise
        out[name] = jnp.asarray(drawn.astype(out[name].dtype))
    for name, factor in factors.items():
        out[name] = (out[name] * factor).astype(out[name].dtype)
    return out
```

```python
import numpy as np

import concourse.bass as bass
import concourse.mybir as mybir
from concourse.alu_op_type import AluOpType as ALU
from contextlib import ExitStack

F32 = mybir.dt.float32
F16 = mybir.dt.float16
BF16 = mybir.dt.bfloat16
I32 = mybir.dt.int32
ACT = mybir.ActivationFunctionType
AX_X = mybir.AxisListType.X

P = 128
SEQS, SEQ, DIM = 4, 1024, 128
HEADS, HEAD = 16, 64
HID = 384
PAIRS = HEADS // 2
BLOCKS = SEQ // P
CH = 512
HB = HID // P
EPS = 1e-5

W_SCALE = 64.0
Q_EVAC = 1.0 / (W_SCALE * 8)
K_EVAC = 1.0 / W_SCALE
ATT_EPS = EPS * (W_SCALE * W_SCALE) ** 2
FFN_DIV = 127.0

def step_groups(i):
    blocks = [(h, t) for h in range(2) for t in range(i + 1)]
    return [blocks[c:c + 4] for c in range(0, len(blocks), 4)]

STEPS = 2 * BLOCKS
GROUPS = [(s, blk) for s in range(STEPS) for blk in step_groups(s % BLOCKS)]
NG = len(GROUPS)
STEP_GROUPS = [[g for g in range(NG) if GROUPS[g][0] == s] for s in range(STEPS)]
LAST_GROUPS = [gs[-1] for gs in STEP_GROUPS]
POOL_GROUPS = [g for g in range(NG) if g % 4 == 1]
RING = 8
LAG = 3

BODY_TASKS = [
    ("q", 0, 0), ("k", 0, 0), ("q", 0, 1), ("k", 0, 1), ("v", 0, 0), ("o", 0, 0), ("v", 0, 1), None,
    ("q", 1, 0), ("k", 1, 0), ("q", 1, 1), ("o", 0, 1), ("k", 1, 1), ("o", 1, 0), ("v", 1, 0), ("v", 1, 1),
    ("o", 1, 1),
]
TASK_NO = {t: n for n, t in enumerate([t for t in BODY_TASKS if t])}
BODY_TASK_COUNT = len(TASK_NO)
W_TASKS = 8 + 3
X_TASKS = SEQS * SEQ // CH
FIRST_TASKS = (("q", 0), ("k", 0), ("q", 1), ("k", 1), ("v", 0), ("v", 1))
PRE_TASKS = W_TASKS + X_TASKS + len(FIRST_TASKS)
STACK_DMAS = 12
FFN_TASKS = 2


def build(nc, x, wq, wk, wv, wo, wg, wu, wd, out):
    ctx = ExitStack()

    def sb(name, shape, dt):
        return ctx.enter_context(nc.sbuf_tensor(name, shape, dt))

    def pb(name, shape, dt):
        return ctx.enter_context(nc.psum_tensor(name, shape, dt))

    def sem(name):
        return ctx.enter_context(nc.semaphore(name))

    with ctx:
        x_sb = sb("x_sb", [P, SEQS * BLOCKS, DIM], F32)
        xT_hi = sb("xT_hi", [P, SEQS * SEQ], F16)
        xT_lo = sb("xT_lo", [P, SEQS * SEQ], F16)
        wT_hi = sb("wT_hi", [P, 4 * PAIRS * P], F16)
        wT_lo = sb("wT_lo", [P, 4 * PAIRS * P], F16)
        fT = sb("fT", [P, 3, HB * P], F16)
        ident = sb("ident", [P, P], F32)
        ident_bf = sb("ident_bf", [P, P], BF16)
        causal = sb("causal", [P, P], BF16)
        zeros = sb("zeros", [P, CH], F16)
        minus_half = sb("minus_half", [P, 8], F32)
        q_hi = sb("q_hi", [P, SEQ], F16)
        q_lo = sb("q_lo", [P, SEQ], F16)
        w_cur = sb("w_cur", [P, 2, 2, 3, P], F16)
        x_cur = sb("x_cur", [P, 2, SEQ], F16)
        k_hi = sb("k_hi", [P, SEQ], F16)
        k_lo = sb("k_lo", [P, SEQ], F16)
        q_st = sb("q_st", [P, 2, 2, SEQ], F16)
        kh_st = sb("kh_st", [P, 2, 2, SEQ], F16)
        kl_st = sb("kl_st", [P, 2, 2, SEQ], F16)
        v_hi = sb("v_hi", [P, 2, SEQ], F16)
        v_lo = sb("v_lo", [P, 2, SEQ], F16)
        probs = sb("probs", [P, 2, 2, SEQ], F32)
        negmax = sb("negmax", [P, 4, 2], F32)
        rowsum = sb("rowsum", [P, 4, 2], F32)
        recip = sb("recip", [P, 4, 2], F32)
        pT_hi = sb("pT_hi", [P, RING, CH], F16)
        pT_lo = sb("pT_lo", [P, RING, CH], F16)
        pT_f = sb("pT_f", [P, 2, CH], F32)
        o_n = sb("o_n", [P, BLOCKS, P], F32)
        stage = sb("stage", [P, 2, CH], F32)
        oT_hi = sb("oT_hi", [P, PAIRS * SEQ], F16)
        oT_lo = sb("oT_lo", [P, PAIRS * SEQ], F16)
        w_raw = oT_hi[:, :].bitcast(F32).rearrange("p (w r d) -> p w r d", w=4, r=PAIRS)
        f_int = kl_st[:, :, :, :].rearrange("p a h c -> p (a h c)")[:, 0:2 * 3 * HB * P].bitcast(I32).rearrange(
            "p (w c) -> p w c", w=3)
        f_raw = oT_lo[:, 0:2 * 3 * HB * P].bitcast(F32).rearrange("p (w c) -> p w c", w=3)
        bst = sb("bst", [P, 8, 6], F32)
        mv = sb("mv", [P, 8, 2], F32)
        veps = sb("veps", [P, 8], F32)
        rstd = sb("rstd", [P, 8], F32)
        yn = sb("yn", [P, 8, DIM], F32)
        x1 = sb("x1", [P, 8, DIM], F32)
        x1n = sb("x1n", [P, 8, DIM], F32)
        x1T_hi = sb("x1T_hi", [P, SEQ], F16)
        x1T_lo = sb("x1T_lo", [P, SEQ], F16)
        t_f = probs[:, 1, 0, :].rearrange("p (a c) -> p a c", a=2)
        g_f = probs[:, 1, 1, :].rearrange("p (a c) -> p a c", a=2)
        h_f = o_n[:, :, :].rearrange("p (a k) c -> p a (k c)", a=2)
        h_hi = sb("h_hi", [P, 2, HB, CH], F16)
        h_lo = sb("h_lo", [P, 2, HB, CH], F16)

        scores = pb("scores", [P, 2, SEQ], F32)
        pT = pb("pT", [P, 2, CH], F32)
        o_ps = pb("o_ps", [P, CH], F32)
        misc = pb("misc", [P, CH], F32)

        dma_w = sem("dma_w")
        dma_f = sem("dma_f")
        dma_x = [sem(f"dma_x{i}") for i in range(4)]
        dma_out = sem("dma_out")
        w_loaded = [sem("w_loaded0"), sem("w_loaded1")]
        x_loaded = sem("x_loaded")
        stacked = [sem("stacked0"), sem("stacked1")]
        const_made = sem("const_made")
        const_ready = sem("const_ready")
        f_cast = sem("f_cast")
        ln_x_stats = sem("ln_x_stats")
        ln_x_aggr = sem("ln_x_aggr")
        ln_x_veps = sem("ln_x_veps")
        ln_x_rstd = sem("ln_x_rstd")
        ln_x_done = sem("ln_x_done")
        bank_filled = sem("bank_filled")
        staged = sem("staged")
        hi_split = sem("hi_split")
        split_done = sem("split_done")
        scores_ready = sem("scores_ready")
        max_ready = sem("max_ready")
        probs_ready = sem("probs_ready")
        pT_filled = sem("pT_filled")
        pT_copied = sem("pT_copied")
        lo_by_vector = sem("lo_by_vector")
        lo_by_pool = sem("lo_by_pool")
        pv_done = sem("pv_done")
        recip_ready = sem("recip_ready")
        o_ready = sem("o_ready")
        y_ready = sem("y_ready")
        st1, ag1, ve1, rs1, yn1_done, x1_done = [sem(n) for n in ("st1", "ag1", "ve1", "rs1", "yn1_done", "x1_done")]
        st2, ag2, ve2, rs2, x1n_done = [sem(n) for n in ("st2", "ag2", "ve2", "rs2", "x1n_done")]
        st3, ag3, ve3, rs3, yn3_done, res_done = [sem(n) for n in ("st3", "ag3", "ve3", "rs3", "yn3_done", "res_done")]
        gu_ready, t_ready, g_ready, h_ready, hh_ready, hl_ready, z_ready = [sem(n) for n in (
            "gu_ready", "t_ready", "g_ready", "h_ready", "hh_ready", "hl_ready", "z_ready")]

        held = sem("held")


        def task_count(n, seq, t):
            return n * BODY_TASK_COUNT + seq * FFN_TASKS + (PRE_TASKS + t + 1)

        pool_before = [len([q for q in POOL_GROUPS if q < g]) for g in range(NG + 1)]
        vec_before = [g - pool_before[g] for g in range(NG + 1)]

        def hi_count(n, seq, pools, tasks):
            return n * (len(POOL_GROUPS) + BODY_TASK_COUNT) + seq * FFN_TASKS + (PRE_HI + pools + tasks)

        PRE_HI = PRE_TASKS - 3

        def group_lo_ready(eng, n, g, before=0):
            if g < 0:
                g += NG
                if g in POOL_GROUPS:
                    eng.wait_ge(lo_by_pool, n * len(POOL_GROUPS) + (pool_before[g + 1] - len(POOL_GROUPS)) + 2)
                else:
                    eng.wait_ge(lo_by_vector, n * (NG - len(POOL_GROUPS)) + (vec_before[g + 1] - vec_before[NG]) + 2)
            elif g in POOL_GROUPS:
                eng.wait_ge(lo_by_pool, n * len(POOL_GROUPS) + pool_before[g + 1] + 2)
            else:
                eng.wait_ge(lo_by_vector, n * (NG - len(POOL_GROUPS)) + vec_before[g + 1] + 2)

        def hold(eng, semaphore, count):
            eng.wait_ge(semaphore, count)
            eng.sem_inc(held, 1)

        block = ctx.enter_context(nc.Block())

        @block.sync
        def _(sp):
            xv = x.rearrange("b (k p) d -> p (b k) d", p=P)
            for i in range(4):
                sp.dma_start(x_sb[:, i * 8:(i + 1) * 8, :], xv[:, i * 8:(i + 1) * 8, :]).then_inc(dma_x[i], 16)
                if i == 0:
                    for w, src in enumerate((wq, wk, wv)):
                        sp.dma_start(w_raw[:, w, :, :],
                                     src.rearrange("(r a) e d -> (a e) r d", a=2)).then_inc(dma_w, 16)
                    sp.dma_start(w_raw[:, 3, :, :], wo.rearrange("d (r c) -> d r c", c=P)).then_inc(dma_w, 16)
                    sp.dma_start(f_int[:, 0, :].rearrange("p (r d) -> p r d", d=DIM),
                                 wg.rearrange("(r p) d -> p r d", p=P)).then_inc(dma_f, 16)
                    sp.dma_start(f_int[:, 1, :].rearrange("p (r d) -> p r d", d=DIM),
                                 wu.rearrange("(r p) d -> p r d", p=P)).then_inc(dma_f, 16)
                    sp.dma_start(f_int[:, 2, :], wd).then_inc(dma_f, 16)

            def stack(buf, q_done, k_done):
                sp.wait_ge(split_done, q_done)
                for h in range(2):
                    rows = slice(h * HEAD, (h + 1) * HEAD)
                    sp.dma_start(q_st[0:HEAD, buf, h, :], q_hi[rows, :]).then_inc(stacked[buf], 16)
                    sp.dma_start(q_st[HEAD:P, buf, h, :], q_lo[rows, :]).then_inc(stacked[buf], 16)
                sp.wait_ge(split_done, k_done)
                for h in range(2):
                    rows = slice(h * HEAD, (h + 1) * HEAD)
                    for dst, src in ((kh_st, k_hi), (kl_st, k_lo)):
                        sp.dma_start(dst[0:HEAD, buf, h, :], src[rows, :]).then_inc(stacked[buf], 16)
                        sp.dma_start(dst[HEAD:P, buf, h, :], src[rows, :]).then_inc(stacked[buf], 16)

            def load_w(buf, pair):
                for part, src in enumerate((wT_hi, wT_lo)):
                    sp.dma_start(w_cur[:, buf, part, :, :],
                                 src[:, 0:3 * PAIRS * P].rearrange("p (w c) -> p w c", w=3)[:, :, bass.ds(pair * P, P)]
                                 ).then_inc(w_loaded[buf], 16)

            def load_x(seq):
                for part, src in enumerate((xT_hi, xT_lo)):
                    sp.dma_start(x_cur[:, part, :], src[:, bass.ds(seq * SEQ, SEQ)]).then_inc(x_loaded, 16)

            sp.wait_ge(split_done, W_TASKS + X_TASKS)
            load_w(0, 1)
            load_x(0)
            stack(0, PRE_TASKS - 3, PRE_TASKS - 2)
            with sp.Fori(0, SEQS) as seq:
                with sp.Fori(0, SEQS) as j:
                    n = sp.snap(seq * 4 + j)
                    hold(sp, bank_filled, task_count(n, seq, -2))
                    load_w(1, (n * 2 + 2) % PAIRS)
                    for u in range(2):
                        if u == 1:
                            hold(sp, bank_filled, task_count(n, seq, TASK_NO[("v", 0, 1)]))
                            load_x(((n * 2 + 2) // PAIRS) % SEQS)
                            load_w(0, (n * 2 + 3) % PAIRS)
                        hold(sp, scores_ready, n * 2 * STEPS + (2 * BLOCKS * u + 1))
                        stack(1 - u, task_count(n, seq, TASK_NO[("q", u, 1)]), task_count(n, seq, TASK_NO[("k", u, 1)]))
                sp.wait_ge(res_done, seq * 2 + 2)
                sp.dma_start(out[bass.ds(seq, 1), :, :].rearrange("b (k p) d -> p (b k) d", p=P),
                             x_sb[:, bass.ds(seq * BLOCKS, BLOCKS), :]).then_inc(dma_out, 16)
            sp.wait_ge(dma_out, 16 * SEQS)

        @block.tensor
        def _(pe):
            mm = nc.tensor.matmul

            def task(count, before, fill):
                if before is not None:
                    pe.wait_ge(staged, before)
                fill().then_inc(bank_filled, 1)

            def transposes(srcs):
                def fill():
                    for c, s in enumerate(srcs):
                        last = nc.tensor.transpose(misc[:, c * P:(c + 1) * P], s, ident[:, :])
                    return last
                return fill

            def proj(kind, half, x_parts, w_parts):
                (xh, xl), (wh, wl) = x_parts, w_parts
                def fill():
                    if kind != "v":
                        tok = slice(half * CH, (half + 1) * CH)
                        mm(misc[:, :], wh, xh[:, tok], start=True, stop=False)
                        mm(misc[:, :], wh, xl[:, tok], start=False, stop=False)
                        return mm(misc[:, :], wl, xh[:, tok], start=False, stop=True)
                    for c in range(4):
                        o = misc[:, c * P:(c + 1) * P]
                        tok = slice(half * CH + c * P, half * CH + (c + 1) * P)
                        mm(o, xh[:, tok], wh, start=True, stop=False)
                        mm(o, xh[:, tok], wl, start=False, stop=False)
                        last = mm(o, xl[:, tok], wh, start=False, stop=True)
                    return last
                return fill

            def step_scores(s, h):
                buf, i = (s // BLOCKS) % 2, s % BLOCKS
                keys = (i + 1) * P
                q = q_st[:, buf, h, i * P:(i + 1) * P]
                for c0 in range(0, keys, CH):
                    c1 = min(c0 + CH, keys)
                    o = scores[:, h, c0:c1]
                    mm(o, q, kh_st[:, buf, h, c0:c1], start=True, stop=False)
                    mm(o, q, kl_st[:, buf, h, c0:c1], start=False, stop=(c1 < keys))
                mm(scores[:, h, i * P:keys], ident_bf[:, :], causal[:, :], start=False,
                   stop=True).then_inc(scores_ready, 1)

            done = 0
            pe.wait_ge(const_ready, 1)
            pe.wait_ge(dma_w, 64)
            for w in range(4):
                for half in range(2):
                    task(None, done if done else None, transposes(
                        [w_raw[:, w, half * 4 + c, :] for c in range(4)]))
                    done += 1
            pe.wait_ge(f_cast, 3)
            for f in range(3):
                task(None, done, transposes([f_raw[:, f, c * P:(c + 1) * P] for c in range(HB)]))
                done += 1
            for g in range(X_TASKS):
                pe.wait_ge(ln_x_done, g + 1)
                task(None, done, transposes([x1n[:, (g % 2) * 4 + c, :] for c in range(4)]))
                done += 1
            pe.wait_ge(split_done, W_TASKS + X_TASKS)
            for kind, half in FIRST_TASKS:
                w = "qkv".index(kind) * PAIRS * P
                task(None, done, proj(kind, half, (xT_hi, xT_lo), (wT_hi[:, w:w + P], wT_lo[:, w:w + P])))
                done += 1
            pe.wait_ge(stacked[0], 16 * STACK_DMAS)
            step_scores(0, 0)
            step_scores(0, 1)

            pe.sem_inc(pv_done, RING)
            pe.sem_inc(lo_by_vector, 2)
            pe.sem_inc(lo_by_pool, 2)
            pe.sem_inc(pT_copied, 2)
            pe.sem_inc(o_ready, 1)
            pe.sem_inc(pT_filled, 1)
            pe.sem_inc(y_ready, 1)
            with pe.Fori(0, SEQS) as seq:
                with pe.Fori(0, SEQS) as j:
                    n = pe.snap(seq * 4 + j)
                    task_no = 0

                    def pv(g):
                        s, blocks = GROUPS[g]
                        buf, i = (s // BLOCKS) % 2, s % BLOCKS
                        group_lo_ready(pe, n, g)
                        if g == STEP_GROUPS[s][0]:
                            pe.wait_ge(o_ready, n * STEPS + (s + 1))
                        for c, (h, t) in enumerate(blocks):
                            o = o_ps[:, h * HEAD:(h + 1) * HEAD]
                            col = slice(c * P, (c + 1) * P)
                            vs = slice(t * P + h * HEAD, t * P + (h + 1) * HEAD)
                            mm(o, pT_hi[:, g % RING, col], v_hi[:, buf, vs], start=(t == 0), stop=False)
                            mm(o, pT_hi[:, g % RING, col], v_lo[:, buf, vs], start=False, stop=False)
                            last = mm(o, pT_lo[:, g % RING, col], v_hi[:, buf, vs], start=False, stop=(t == i))
                        last.then_inc(pv_done, 1)

                    for s in range(STEPS):
                        u, i = s // BLOCKS, s % BLOCKS
                        nxt = s + 1
                        if nxt % BLOCKS == 0:
                            pe.wait_ge(stacked[1 - u], n * 16 * STACK_DMAS + (u + 1) * 16 * STACK_DMAS)
                        pe.wait_ge(probs_ready, n * 2 * STEPS + (2 * s + 1))
                        step_scores(nxt, 0)
                        if i in (0, 4):
                            pe.wait_ge(split_done, task_count(n, seq, TASK_NO[("v", 0, i // 4)] if u else i // 4 - 2))
                        for g in STEP_GROUPS[s]:
                            pe.wait_ge(probs_ready, n * 2 * STEPS + (2 * s + 1 + GROUPS[g][1][-1][0]))
                            prev = g - 2
                            if (prev % NG) in POOL_GROUPS:
                                pe.wait_ge(pT_copied, n * NG + (prev + 1 + 2))
                            else:
                                group_lo_ready(pe, n, prev)
                            for c, (h, t) in enumerate(GROUPS[g][1]):
                                last = nc.tensor.transpose(pT[:, g % 2, c * P:(c + 1) * P],
                                                           probs[:, s % 2, h, t * P:(t + 1) * P], ident[:, :])
                            last.then_inc(pT_filled, 1)
                            if g >= LAG:
                                pv(g - LAG)
                            if g == STEP_GROUPS[s][:2][-1]:
                                pe.wait_ge(probs_ready, n * 2 * STEPS + (2 * s + 2))
                                step_scores(nxt, 1)
                                t = BODY_TASKS[s]
                                if t:
                                    kind, uu, half = t
                                    if kind == "o":
                                        pe.wait_ge(o_ready, n * STEPS + (uu * BLOCKS + half * 4 + 4 + 1))
                                        fill = transposes([o_n[:, half * 4 + c, :] for c in range(4)])
                                    else:
                                        w = "qkv".index(kind)
                                        if (kind, half) == ("q", 0):
                                            pe.wait_ge(w_loaded[u], (n + 1) * 32)
                                            pe.wait_ge(x_loaded, (n + (u + 1)) * 32)
                                        fill = proj(kind, half, (x_cur[:, 0, :], x_cur[:, 1, :]),
                                                    (w_cur[:, u, 0, w, :], w_cur[:, u, 1, w, :]))
                                    task(None, task_count(n, seq, task_no - 1), fill)
                                    task_no += 1
                    for g in range(NG - LAG, NG):
                        pv(g)
                    pe.wait_ge(o_ready, n * STEPS + (STEPS + 1))
                    task(None, task_count(n, seq, task_no - 1), transposes([o_n[:, 4 + c, :] for c in range(4)]))
                    task_no += 1
                    assert task_no == BODY_TASK_COUNT

                nb = pe.snap(seq * 4 + 4)
                pe.wait_ge(split_done, nb * BODY_TASK_COUNT + seq * FFN_TASKS + PRE_TASKS)
                pe.wait_ge(probs_ready, nb * 2 * STEPS + 2)
                for half in range(2):
                    for c in range(4):
                        tok = half * CH + c * P
                        o = scores[:, 0, half * CH + c * P:half * CH + (c + 1) * P]
                        for r in range(PAIRS):
                            w = slice((3 * PAIRS + r) * P, (3 * PAIRS + r + 1) * P)
                            a = slice(r * SEQ + tok, r * SEQ + tok + P)
                            mm(o, oT_hi[:, a], wT_hi[:, w], start=(r == 0), stop=False)
                            mm(o, oT_hi[:, a], wT_lo[:, w], start=False, stop=False)
                            last = mm(o, oT_lo[:, a], wT_hi[:, w], start=False, stop=(r == PAIRS - 1))
                    last.then_inc(y_ready, 1)
                for half in range(2):
                    pe.wait_ge(x1n_done, seq * 2 + half + 1)
                    task(None, nb * BODY_TASK_COUNT + seq * FFN_TASKS + (PRE_TASKS + half),
                         transposes([x1n[:, half * 4 + c, :] for c in range(4)]))
                for c in range(2 * HB):
                    half, hb = c // HB, c % HB
                    bank = 1 - c % 2
                    if hb == 0:
                        pe.wait_ge(split_done, nb * BODY_TASK_COUNT + seq * FFN_TASKS + (PRE_TASKS + half + 1))
                    if c >= 2:
                        pe.wait_ge(h_ready, seq * 2 * HB + c - 1)
                    elif c == 1:
                        pe.wait_ge(yn1_done, seq * 2 + 2)
                    for m in range(2):
                        o = scores[:, bank, m * CH:(m + 1) * CH]
                        w = fT[:, m, hb * P:(hb + 1) * P]
                        mm(o, w, x1T_hi[:, half * CH:(half + 1) * CH], start=True, stop=False)
                        last = mm(o, w, x1T_lo[:, half * CH:(half + 1) * CH], start=False, stop=True)
                    last.then_inc(gu_ready, 1)
                for half in range(2):
                    pe.wait_ge(hl_ready, seq * 2 * HB + (half + 1) * HB)
                    for c in range(4):
                        o = pT[:, half, c * P:(c + 1) * P]
                        col = slice(c * P, (c + 1) * P)
                        for hb in range(HB):
                            w = fT[:, 2, hb * P:(hb + 1) * P]
                            mm(o, h_hi[:, half, hb, col], w, start=(hb == 0), stop=False)
                            last = mm(o, h_lo[:, half, hb, col], w, start=False, stop=(hb == HB - 1))
                    last.then_inc(z_ready, 1)
                pe.wait_ge(yn3_done, seq * 2 + 2)

        @block.scalar
        def _(act):
            def copy_task(count_filled, slot, cols, scale, free):
                act.wait_ge(bank_filled, count_filled)
                if free is not None:
                    act.wait_ge(split_done, free)
                nc.scalar.activation(stage[:, slot, 0:cols], misc[:, 0:cols], ACT.Copy, scale=scale).then_inc(staged, 1)

            def task_copy(n, seq, t, kind):
                scale = {"q": Q_EVAC, "k": K_EVAC, "v": 1.0, "o": 1.0}[kind]
                copy_task(task_count(n, seq, t), (PRE_TASKS + t) % 2, CH, scale, task_count(n, seq, t - 2))

            def exp(n, s, first=False):
                def head(h):
                    i = s % BLOCKS
                    keys = (i + 1) * P
                    if first:
                        act.wait_ge(max_ready, h + 1)
                    else:
                        act.wait_ge(max_ready, n * 2 * STEPS + (2 * s + h + 1))
                        if h == 0:
                            act.wait_ge(pT_filled, n * NG + (STEP_GROUPS[s - 2][-1] + 1 + 1 if s >= 2 else 1))
                    nc.scalar.activation(probs[:, s % 2, h, 0:keys], scores[:, h, 0:keys], ACT.Exp,
                                         bias=negmax[:, s % 4, h:h + 1],
                                         accum_out=rowsum[:, s % 4, h:h + 1]).then_inc(probs_ready, 1)
                return head

            done = 0
            for w in range(4):
                for half in range(2):
                    copy_task(done + 1, done % 2, CH, W_SCALE, done - 1 if done >= 2 else None)
                    done += 1
            for f in range(3):
                copy_task(done + 1, done % 2, HB * P, 1.0, done - 1)
                done += 1
            for g in range(X_TASKS):
                copy_task(done + 1, done % 2, CH, 1.0, done - 1)
                done += 1
            for kind, half in FIRST_TASKS:
                scale = {"q": Q_EVAC, "k": K_EVAC, "v": 1.0}[kind]
                copy_task(done + 1, done % 2, CH, scale, done - 1)
                done += 1
            first = exp(None, 0, first=True)
            first(0)
            first(1)

            with act.Fori(0, SEQS) as seq:
                with act.Fori(0, SEQS) as j:
                    n = act.snap(seq * 4 + j)
                    task_no = 0

                    def group_copy(g):
                        cols = len(GROUPS[g][1]) * P
                        act.wait_ge(pT_filled, n * NG + (g + 1 + 1))
                        if g in POOL_GROUPS:
                            k = pool_before[g]
                            act.wait_ge(lo_by_pool, n * len(POOL_GROUPS) + (k + 1))
                            nc.scalar.copy(pT_f[:, k % 2, 0:cols], pT[:, g % 2, 0:cols]).then_inc(pT_copied, 1)
                        else:
                            act.wait_ge(pv_done, n * NG + (g + 1))
                            nc.scalar.copy(pT_hi[:, g % RING, 0:cols], pT[:, g % 2, 0:cols]).then_inc(pT_copied, 1)

                    for s in range(STEPS):
                        nxt = exp(n, s + 1)
                        gs = STEP_GROUPS[s]
                        for g in gs[:2]:
                            group_copy(g)
                        nxt(0)
                        for g in gs[2:]:
                            group_copy(g)
                        nxt(1)
                        if BODY_TASKS[s]:
                            task_copy(n, seq, task_no, BODY_TASKS[s][0])
                            task_no += 1
                    task_copy(n, seq, task_no, "o")
                    task_no += 1

                nb = act.snap(seq * 4 + 4)
                for half in range(2):
                    t = nb * BODY_TASK_COUNT + seq * FFN_TASKS + (PRE_TASKS + half)
                    copy_task(t + 1, (PRE_TASKS + half) % 2, CH, 1.0, t - 1)
                for c in range(2 * HB):
                    act.wait_ge(gu_ready, seq * 2 * HB + c + 1)
                    if c >= 2:
                        act.wait_ge(g_ready, seq * 2 * HB + c - 1)
                    nc.scalar.activation(t_f[:, c % 2, :], scores[:, 1 - c % 2, 0:CH], ACT.Tanh,
                                         scale=0.5 / FFN_DIV).then_inc(t_ready, 1)

        @block.vector
        def _(dve):
            tt, ts = nc.vector.tensor_tensor, nc.vector.tensor_scalar

            def row_max(n, s):
                def head(h):
                    keys = (s % BLOCKS + 1) * P
                    if n is None:
                        dve.wait_ge(scores_ready, h + 1)
                    else:
                        dve.wait_ge(scores_ready, n * 2 * STEPS + (2 * s + h + 1))
                    nc.vector.tensor_reduce(negmax[:, s % 4, h:h + 1], scores[:, h, 0:keys], AX_X, ALU.max,
                                            negate=True).then_inc(max_ready, 1)
                return head

            for g in range(X_TASKS):
                if g % 2 == 0:
                    dve.wait_ge(dma_x[g // 2], 16)
                for c in range(4):
                    last = nc.vector.bn_stats(bst[:, (g % 2) * 4 + c, :], x_sb[:, g * 4 + c, :])
                last.then_inc(ln_x_stats, 1)
                dve.wait_ge(ln_x_stats, g + 1)
                if g >= 2:
                    dve.wait_ge(ln_x_rstd, g - 1)
                for c in range(4):
                    last = nc.vector.bn_aggr(mv[:, (g % 2) * 4 + c, :], bst[:, (g % 2) * 4 + c, :])
                last.then_inc(ln_x_aggr, 1)
                dve.wait_ge(ln_x_rstd, g + 1)
                dve.wait_ge(ln_x_aggr, g + 1)
                if g >= 2:
                    dve.wait_ge(bank_filled, W_TASKS + g - 1)
                for c in range(4):
                    k = (g % 2) * 4 + c
                    last = ts(x1n[:, k, :], x_sb[:, g * 4 + c, :], mv[:, k, 0:1], rstd[:, k:k + 1],
                              ALU.subtract, ALU.mult)
                last.then_inc(ln_x_done, 1)
            row_max(None, 0)(0)
            row_max(None, 0)(1)

            with dve.Fori(0, SEQS) as seq:
                with dve.Fori(0, SEQS) as j:
                    n = dve.snap(seq * 4 + j)

                    def group_lo(g):
                        if g in POOL_GROUPS:
                            return
                        cols = len(GROUPS[g][1]) * P
                        dve.wait_ge(pT_copied, n * NG + (g + 1 + 2))
                        tt(pT_lo[:, g % RING, 0:cols], pT[:, g % 2, 0:cols], pT_hi[:, g % RING, 0:cols],
                           ALU.subtract).then_inc(lo_by_vector, 1)

                    def reciprocal(s):
                        dve.wait_ge(probs_ready, n * 2 * STEPS + (2 * s + 2))
                        nc.vector.reciprocal(recip[:, s % 4, :], rowsum[:, s % 4, :]).then_inc(recip_ready, 1)

                    def normalise(s):
                        dve.wait_ge(recip_ready, n * STEPS + (s + 1))
                        dve.wait_ge(pv_done, n * NG + (STEP_GROUPS[s][-1] + 1 + RING))
                        if s % 4 == 0:
                            u, half = s // BLOCKS, (s % BLOCKS) // 4
                            before = (0, half) if u == 1 else None
                            if before:
                                dve.wait_ge(bank_filled, task_count(n, seq, TASK_NO[("o",) + before]))
                            else:
                                dve.wait_ge(bank_filled, task_count(n, seq, -1))
                        tt(o_n[:, s % BLOCKS, :].rearrange("p (h e) -> p h e", h=2),
                           o_ps[:, 0:P].rearrange("p (h e) -> p h e", h=2),
                           recip[:, s % 4, :].unsqueeze(2).to_broadcast([P, 2, HEAD]), ALU.mult).then_inc(o_ready, 1)

                    for s in range(STEPS):
                        nxt = row_max(n, s + 1)
                        nxt(0)
                        reciprocal(s)
                        for g in STEP_GROUPS[s]:
                            if g >= LAG and g - LAG in LAST_GROUPS:
                                normalise(GROUPS[g - LAG][0])
                            group_lo(g)
                            if g == STEP_GROUPS[s][:2][-1]:
                                nxt(1)
                    for g in range(NG - LAG, NG):
                        if g in LAST_GROUPS:
                            normalise(GROUPS[g][0])

                def layernorm_stats(count, stats, aggr, k0, src, free=None):
                    for c in range(4):
                        last = nc.vector.bn_stats(bst[:, k0 + c, :], src(c))
                    last.then_inc(stats, 1)
                    hold(dve, stats, count)
                    for c in range(4):
                        last = nc.vector.bn_aggr(mv[:, k0 + c, :], bst[:, k0 + c, :])
                    last.then_inc(aggr, 1)

                def apply_norm(done, dst, k0, src):
                    for c in range(4):
                        k = k0 + c
                        last = ts(dst[:, k, :], src(c), mv[:, k, 0:1], rstd[:, k:k + 1], ALU.subtract, ALU.mult)
                    last.then_inc(done, 1)

                def y_block(half):
                    return lambda c: scores[:, 0, half * CH + c * P:half * CH + (c + 1) * P]

                for half in range(2):
                    dve.wait_ge(y_ready, seq * 2 + (half + 1 + 1))
                    layernorm_stats(seq * 2 + half + 1, st1, ag1, half * 4, y_block(half))
                for half in range(2):
                    dve.wait_ge(rs1, seq * 2 + half + 1)
                    dve.wait_ge(ag1, seq * 2 + half + 1)
                    apply_norm(yn1_done, yn, half * 4, y_block(half))
                for half in range(2):
                    dve.wait_ge(x1_done, seq * 2 + half + 1)
                    layernorm_stats(seq * 2 + half + 1, st2, ag2, half * 4, lambda c: x1[:, half * 4 + c, :])
                for half in range(2):
                    dve.wait_ge(rs2, seq * 2 + half + 1)
                    dve.wait_ge(ag2, seq * 2 + half + 1)
                    apply_norm(x1n_done, x1n, half * 4, lambda c: x1[:, half * 4 + c, :])
                for c in range(2 * HB):
                    k = seq * 2 * HB + c + 1
                    bank = 1 - c % 2
                    dve.wait_ge(t_ready, k)
                    nc.vector.scalar_tensor_tensor(out=g_f[:, c % 2, :], in0=t_f[:, c % 2, :], scalar=1.0,
                                                   in1=scores[:, bank, 0:CH], op0=ALU.add,
                                                   op1=ALU.mult).then_inc(g_ready, 1)
                    dve.wait_ge(g_ready, k)
                    if c >= 2:
                        dve.wait_ge(hl_ready, k - 2)
                    nc.vector.scalar_tensor_tensor(out=h_f[:, c % 2, :], in0=scores[:, bank, CH:2 * CH],
                                                   scalar=0.5 / (FFN_DIV * FFN_DIV), in1=g_f[:, c % 2, :],
                                                   op0=ALU.mult, op1=ALU.mult).then_inc(h_ready, 1)

                def z_block(half):
                    return lambda c: pT[:, half, c * P:(c + 1) * P]

                for half in range(2):
                    dve.wait_ge(z_ready, seq * 2 + half + 1)
                    layernorm_stats(seq * 2 + half + 1, st3, ag3, half * 4, z_block(half))
                for half in range(2):
                    dve.wait_ge(rs3, seq * 2 + half + 1)
                    dve.wait_ge(ag3, seq * 2 + half + 1)
                    apply_norm(yn3_done, yn, half * 4, z_block(half))

        @block.gpsimd
        def _(pool):
            gp = nc.gpsimd
            hi_done = [0]

            gp.memset(ident[:, :], 0.0)
            gp.memset(ident_bf[:, :], 0.0)
            gp.memset(causal[:, :], 0.0)
            gp.memset(zeros[:, :], 0.0)
            gp.memset(minus_half[:, :], -0.5).then_inc(const_made, 1)
            pool.wait_ge(const_made, 1)
            for m in (ident, ident_bf):
                gp.affine_select(out=m[:, :], in_=m[:, :], compare_op=ALU.not_equal, fill=1.0, base=0,
                                 pattern=[[-1, P]], channel_multiplier=1)
            gp.affine_select(out=causal[:, :], in_=causal[:, :], compare_op=ALU.is_ge, fill=-1e30, base=0,
                             pattern=[[-1, P]], channel_multiplier=1).then_inc(const_ready, 1)
            pool.wait_ge(dma_f, 48)
            for f in range(3):
                gp.tensor_copy(f_raw[:, f, :], f_int[:, f, :]).then_inc(f_cast, 1)

            def split(src, hi, lo, hi_count, moving=False):
                pool.sem_inc(held, 1)
                if moving:
                    gp.tensor_tensor(hi, src, zeros[:, :], ALU.add).then_inc(hi_split, 1)
                else:
                    gp.tensor_scalar(hi, src, 1.0, 0.0, ALU.mult, ALU.add).then_inc(hi_split, 1)
                pool.wait_ge(hi_split, hi_count)
                return gp.tensor_tensor(lo, src, hi, ALU.subtract)

            def make_rstd(count, aggr, veps_sem, rs_sem, k0, eps):
                hold(pool, aggr, count)
                gp.tensor_scalar(veps[:, k0:k0 + 4], mv[:, k0:k0 + 4, 1], eps, None, ALU.add).then_inc(veps_sem, 1)
                pool.wait_ge(veps_sem, count)
                gp.tensor_tensor(rstd[:, k0:k0 + 4], veps[:, k0:k0 + 4], minus_half[:, 0:4],
                                 ALU.pow).then_inc(rs_sem, 1)

            done = 0
            for w in range(4):
                for half in range(2):
                    pool.wait_ge(staged, done + 1)
                    dst = slice((w * 2 + half) * CH, (w * 2 + half + 1) * CH)
                    split(stage[:, done % 2, :], wT_hi[:, dst], wT_lo[:, dst], done + 1).then_inc(split_done, 1)
                    done += 1
            hi_done = done
            for f in range(3):
                pool.wait_ge(staged, done + 1)
                gp.tensor_scalar(fT[:, f, :], stage[:, done % 2, 0:HB * P], 1.0, 0.0, ALU.mult,
                                 ALU.add).then_inc(split_done, 1)
                done += 1
            for g in range(X_TASKS + 1):
                if g < X_TASKS:
                    make_rstd(g + 1, ln_x_aggr, ln_x_veps, ln_x_rstd, (g % 2) * 4, EPS)
                if g >= 1:
                    pool.wait_ge(staged, done + 1)
                    dst = slice((g - 1) * CH, g * CH)
                    hi_done += 1
                    split(stage[:, done % 2, :], xT_hi[:, dst], xT_lo[:, dst], hi_done).then_inc(split_done, 1)
                    done += 1
            for kind, half in FIRST_TASKS:
                pool.wait_ge(staged, done + 1)
                hi, lo = {"q": (q_hi, q_lo), "k": (k_hi, k_lo), "v": (v_hi[:, 0, :], v_lo[:, 0, :])}[kind]
                dst = slice(half * CH, (half + 1) * CH)
                hi_done += 1
                split(stage[:, done % 2, :], hi[:, dst], lo[:, dst], hi_done).then_inc(split_done, 1)
                done += 1
            assert done == PRE_TASKS and hi_done == PRE_HI

            with pool.Fori(0, SEQS) as seq:
                with pool.Fori(0, SEQS) as j:
                    n = pool.snap(seq * 4 + j)
                    task_no = 0
                    pools = 0

                    def split_task(t, pools):
                        kind, uu, half = [b for b in BODY_TASKS if b][t]
                        pool.wait_ge(staged, task_count(n, seq, t))
                        src = stage[:, (PRE_TASKS + t) % 2, :]
                        if kind == "o":
                            if uu == 0:
                                pool.wait_ge(y_ready, seq * 2 + 1)
                            dst = bass.ds(j * 2 * SEQ + (uu * SEQ + half * CH), CH)
                            hi, lo = oT_hi[:, dst], oT_lo[:, dst]
                        else:
                            dst = slice(half * CH, (half + 1) * CH)
                            if kind == "v":
                                hi, lo = v_hi[:, 1 - uu, dst], v_lo[:, 1 - uu, dst]
                                if half == 0:
                                    pool.wait_ge(pv_done, n * NG + (NG // 2 * uu + RING))
                            else:
                                a, b = {"q": (q_hi, q_lo), "k": (k_hi, k_lo)}[kind]
                                hi, lo = a[:, dst], b[:, dst]
                                if half == 0:
                                    pool.wait_ge(stacked[uu], (n + 1) * 16 * STACK_DMAS)
                        split(src, hi, lo, hi_count(n, seq, pools, t + 1), kind == "o").then_inc(split_done, 1)

                    for s in range(STEPS):
                        for g in STEP_GROUPS[s]:
                            if g in POOL_GROUPS:
                                cols = len(GROUPS[g][1]) * P
                                pool.wait_ge(pT_copied, n * NG + (g + 1 + 2))
                                pool.wait_ge(pv_done, n * NG + (g + 1))
                                pools += 1
                                split(pT_f[:, (pools - 1) % 2, 0:cols], pT_hi[:, g % RING, 0:cols],
                                      pT_lo[:, g % RING, 0:cols],
                                      hi_count(n, seq, pools, task_no)).then_inc(lo_by_pool, 1)
                        if BODY_TASKS[s]:
                            split_task(task_no, pools)
                            task_no += 1
                    split_task(task_no, pools)
                    task_no += 1

                nb = pool.snap(seq * 4 + 4)
                for half in range(2):
                    make_rstd(seq * 2 + half + 1, ag1, ve1, rs1, half * 4, ATT_EPS)
                for half in range(2):
                    pool.wait_ge(yn1_done, seq * 2 + half + 1)
                    gp.tensor_tensor(x1[:, half * 4:half * 4 + 4, :],
                                     x_sb[:, bass.ds(seq * 8 + half * 4, 4), :],
                                     yn[:, half * 4:half * 4 + 4, :], ALU.add).then_inc(x1_done, 1)
                for half in range(2):
                    make_rstd(seq * 2 + half + 1, ag2, ve2, rs2, half * 4, EPS)
                for half in range(2):
                    pool.wait_ge(staged, nb * BODY_TASK_COUNT + seq * FFN_TASKS + (PRE_TASKS + half + 1))
                    dst = slice(half * CH, (half + 1) * CH)
                    split(stage[:, (PRE_TASKS + half) % 2, :], x1T_hi[:, dst], x1T_lo[:, dst],
                          hi_count(nb, seq, 0, half + 1)).then_inc(split_done, 1)
                for c in range(2 * HB):
                    half, hb = c // HB, c % HB
                    k = seq * 2 * HB + c + 1
                    hold(pool, h_ready, k)
                    gp.tensor_scalar(h_hi[:, half, hb, :], h_f[:, c % 2, :], 1.0, 0.0, ALU.mult,
                                     ALU.add).then_inc(hh_ready, 1)
                    pool.wait_ge(hh_ready, k)
                    gp.tensor_tensor(h_lo[:, half, hb, :], h_f[:, c % 2, :], h_hi[:, half, hb, :],
                                     ALU.subtract).then_inc(hl_ready, 1)
                for half in range(2):
                    make_rstd(seq * 2 + half + 1, ag3, ve3, rs3, half * 4, EPS * FFN_DIV * FFN_DIV)
                for half in range(2):
                    hold(pool, yn3_done, seq * 2 + half + 1)
                    gp.tensor_tensor(x_sb[:, bass.ds(seq * BLOCKS + half * 4, 4), :], x1[:, half * 4:half * 4 + 4, :],
                                     yn[:, half * 4:half * 4 + 4, :], ALU.add).then_inc(res_done, 1)


_INS = ["L0_attn_x", "L0_attn_wq", "L0_attn_wk", "L0_attn_wv", "L0_attn_wo",
        "L0_ffn_w_gate", "L0_ffn_w_up", "L0_ffn_w_down"]


def kernel(**inputs):
    import concourse.bacc as _bacc
    from concourse.bass_utils import run_bass_kernel_spmd as _run

    nc = _bacc.Bacc("TRN2", target_bir_lowering=False, num_devices=1)
    arrays, args = {}, []
    for name in _INS:
        a = np.ascontiguousarray(inputs[name])
        arrays[f"in_{name}"] = a
        args.append(nc.dram_tensor(f"in_{name}", a.shape, mybir.dt.from_np(a.dtype), kind="ExternalInput").ap())
    out = nc.dram_tensor("out_0", (SEQS, SEQ, DIM), F32, kind="ExternalOutput").ap()
    build(nc, *args, out)
    r = _run(nc, [arrays], core_ids=[0])
    return r.results[0]["out_0"]
```
